# Optimizing a Trainium2 kernel written in Bass

```python
import numpy as np
import jax
import jax.numpy as jnp

def _softmax(x, axis=-1):
    return jax.nn.softmax(x, axis=axis)

def _gelu(x):
    return jax.nn.gelu(x, approximate=True)

def _silu(x):
    return jax.nn.silu(x)

def _sigmoid(x):
    return jax.nn.sigmoid(x)

def _layernorm(x, axis=-1, eps=1e-05):
    m = jnp.mean(x, axis=axis, keepdims=True)
    v = jnp.var(x, axis=axis, keepdims=True)
    return (x - m) / jnp.sqrt(v + eps)

def _scatter_add(tgt, idx, src, axis=0):
    return tgt.at[idx].add(src)

def _segment_sum(src, seg, n):
    return jax.ops.segment_sum(src, seg, n)
kernel_name = 'mk_rec_standalone_d1_rec_r8_53cfa7'

def setup_inputs(seed: int=0):
    np.random.seed(seed)
    _w = jnp.asarray

    def _rec_inputs():
        import jax
        import jax.numpy as jnp
        _rk = jax.random.key(seed)
        r_x = -0.000392918 + 0.999932 * jax.random.normal(jax.random.fold_in(_rk, 1), (2048, 32, 64), jnp.float32)
        return r_x
    r_x = _rec_inputs()

    def _L0_rec_setup():
        import jax, jax.numpy as jnp
        import numpy as np
        BATCH = 1024
        NUM_FIELDS = 32
        EMBED_DIM = 64
        NUM_IX = NUM_FIELDS * (NUM_FIELDS - 1) // 2
        key = jax.random.key(seed)
        kx, kk = jax.random.split(key)
        x = jax.random.normal(kx, (BATCH, NUM_FIELDS, EMBED_DIM), dtype=jnp.float32)
        fan = EMBED_DIM + EMBED_DIM
        limit = float(np.sqrt(6.0 / fan))
        kernel = jax.random.uniform(kk, (EMBED_DIM, NUM_IX, EMBED_DIM), dtype=jnp.float32, minval=-limit, maxval=limit)
        return {'x': x, 'kernel': kernel}
    _L0_rec_all = _L0_rec_setup()
    _L0_rec_in = {k: v for k, v in _L0_rec_all.items() if k in ('kernel',)}
    del _L0_rec_all
    return {'r_x': r_x, 'L0_rec_kernel': _L0_rec_in['kernel']}

def reference(r_x, L0_rec_kernel):
    import jax
    import jax.numpy as jnp

    def _L0_rec_ref(x, kernel):
        import jax, jax.numpy as jnp
        import numpy as np
        BATCH = 1024
        NUM_FIELDS = 32
        EMBED_DIM = 64
        NUM_IX = NUM_FIELDS * (NUM_FIELDS - 1) // 2
        num_fields = x.shape[1]
        row, col = np.triu_indices(num_fields, k=1)
        p = x[:, row]
        q = x[:, col]
        out = jnp.einsum('bni,oni,bno->bn', p, kernel, q)
        return out
    y = _L0_rec_ref(r_x, L0_rec_kernel)
    return y

_drawn_inputs = setup_inputs


def setup_inputs(seed=0):
    import zlib

    import numpy as np

    out = dict(_drawn_inputs(seed))
    spreads = {}
    factors = {}
    for name, (base, spread) in spreads.items():
        noise = np.random.default_rng([zlib.crc32(name.encode()), seed]).standard_normal(out[name].shape)
        drawn = base * np.exp(spread * noise) if base else spread * noise
        out[name] = jnp.asarray(drawn.astype(out[name].dtype))
    for name, factor in factors.items():
        out[name] = (out[name] * factor).astype(out[name].dtype)
    return out
```

```python
from contextlib import ExitStack

import concourse.bass as bass
from concourse import mybir

BATCH = 2048
FIELDS = 32
E = 64
PAIRS = FIELDS * (FIELDS - 1) // 2
XT = FIELDS // 2
ITERS = XT // 2
HALF_TILES = XT - 1
TILES = 2 * HALF_TILES + 1
SINGLE = HALF_TILES
SLOTS = TILES + 1
BLK = 4
BLOCKS = SLOTS // BLK
KRING = 4
CH = 512
CHUNKS = BATCH // CH
HB = BATCH // 2
TBUF, PBUF = 3, 4
HALVES = 2 * TILES
GROUP = 16
OUTS = 2 * ITERS


def slot_of(tile):
    return tile if tile <= SINGLE else tile + 1


def last_tile_of_block(b):
    return max(t for t in range(TILES) if (SINGLE + 1 if t == SINGLE else slot_of(t)) // BLK >= b
               and slot_of(t) // BLK <= b)


def second_row(place, j):
    most = j if isinstance(j, int) else ITERS - 2
    return 0 if place + most < HALF_TILES else (j + (place + 1)) // (HALF_TILES + 1)


def before(local, bufs):
    if local >= bufs:
        return 0, local - bufs
    return 1, max(l for l in range(HALVES) if l % bufs == local % bufs)


def build(nc, x, w, out):
    f32, f32r = mybir.dt.float32, mybir.dt.float32r
    ALU, ACT = mybir.AluOpType, mybir.ActivationFunctionType

    ctx = ExitStack()
    with ctx:
        def sb(name, shape, dt=f32):
            return ctx.enter_context(nc.sbuf_tensor(name, shape, dt))

        def sem(name):
            return ctx.enter_context(nc.semaphore(name))

        xq = sb("xq", [128, XT, BATCH])
        stack = sb("stack", [128, 4 * BATCH], f32r)
        kraw = sb("kraw", [128, KRING, BLK * 128])
        khi = sb("khi", [128, KRING, BLK * 128], f32r)
        klo = sb("klo", [128, KRING, BLK * 128], f32r)
        prod = sb("prod", [128, PBUF, HB])
        sums = sb("sums", [128, 2, CH])
        ones = sb("ones", [128, 64])
        tps = ctx.enter_context(nc.psum_tensor("tps", [128, TBUF, HB], f32))
        rps = ctx.enter_context(nc.psum_tensor("rps", [128, 2, CH], f32))

        first_x = list(range(ITERS - 1, XT))
        later_x = list(range(ITERS - 2, -1, -1))
        x_loaded = {k: sem(f"x_loaded_{k}") for k in first_x}
        x_rest_loaded = sem("x_rest_loaded")
        kraw_loaded = [sem(f"kraw_loaded_{n}") for n in range(KRING)]
        ones_zeroed = sem("ones_zeroed")
        ones_ready = sem("ones_ready")
        khi_ready = sem("khi_ready")
        klo_ready = sem("klo_ready")
        xtmp_ready = sem("xtmp_ready")
        xhi_ready = sem("xhi_ready")
        xlo_ready = sem("xlo_ready")
        t_ready = sem("t_ready")
        prod_ready = sem("prod_ready")
        tile_summed = sem("tile_summed")
        sums_copied = sem("sums_copied")
        sums_stored = sem("sums_stored")

        def row_of(engine, i):
            return ITERS - 1 - i if isinstance(i, int) else engine.snap(i * -1 + (ITERS - 1))

        block = ctx.enter_context(nc.Block())

        @block.sync
        def _(sp):
            def load_round(i, first):
                for b in range(BLOCKS):
                    n = b % KRING
                    if not (first and b < KRING):
                        sp.wait_ge(klo_ready, BLOCKS * i + b - KRING + 1)
                    for top in (0, E):
                        sp.dma_start(kraw[top:top + E, n, :], w[i, b]).then_inc(kraw_loaded[n], 16)

            load_round(0, True)
            with sp.Fori(1, ITERS) as i:
                load_round(i, False)

        @block.scalar
        def _(act):
            for k in first_x:
                act.dma_start(xq[:, k, :], x[k]).then_inc(x_loaded[k], 16)
            for k in later_x:
                act.dma_start(xq[:, k, :], x[k]).then_inc(x_rest_loaded, 16)

            def stacks(i, j, odd, first):
                src = slice(E * odd, E * odd + E)
                dst = slice(E * (1 - odd), E * (1 - odd) + E)
                if not first:
                    act.wait_ge(t_ready, HALVES * i if odd else HALVES * (i - 1) + 2 * (SINGLE + 1))
                for n, k in enumerate((j, ITERS + i)):
                    if first and not odd:
                        act.wait_ge(x_loaded[k], 16)
                    for h in range(2):
                        at = (2 * odd + n) * BATCH + h * HB
                        source = xq[src, k, h * HB:(h + 1) * HB]
                        nc.scalar.activation(stack[src, at:at + HB], source, ACT.Copy).then_inc(xtmp_ready, 1)
                        nc.scalar.activation(stack[dst, at:at + HB], source, ACT.Copy).then_inc(xhi_ready, 1)

            def weights(i, b, first):
                n = b % KRING
                act.wait_ge(kraw_loaded[n], 32 * (BLOCKS // KRING * i + b // KRING + 1))
                if b >= KRING:
                    act.wait_ge(t_ready, HALVES * i + 2 * (last_tile_of_block(b - KRING) + 1))
                elif not first:
                    act.wait_ge(t_ready, HALVES * (i - 1) + 2 * (last_tile_of_block(b + BLOCKS - KRING) + 1))
                nc.scalar.activation(khi[:, n, :], kraw[:, n, :], ACT.Copy).then_inc(khi_ready, 1)

            def store_sums(i, odd, first):
                act.wait_ge(tile_summed, TILES * i + (TILES if odd else GROUP))
                if not first:
                    act.wait_ge(sums_stored, 16 * (2 * i + odd))
                nc.scalar.activation(sums[:, odd, :], rps[:, odd, :], ACT.Copy).then_inc(sums_copied, 1)
                act.wait_ge(sums_copied, 2 * i + odd + 1)
                act.dma_start(out[2 * i + odd], sums[:, odd, :]).then_inc(sums_stored, 16)

            stacks(0, ITERS - 1, 0, True)
            for b in range(BLOCKS):
                weights(0, b, True)
                if b == KRING - 1:
                    stacks(0, ITERS - 1, 1, True)
            store_sums(0, 0, True)
            act.wait_ge(x_rest_loaded, 16 * len(later_x))
            with act.Fori(1, ITERS) as i:
                j = row_of(act, i)
                stacks(i, j, 0, False)
                for b in range(KRING):
                    weights(i, b, False)
                store_sums(i - 1, 1, False)
                stacks(i, j, 1, False)
                for b in range(KRING, BLOCKS):
                    weights(i, b, False)
                store_sums(i, 0, False)
            store_sums(ITERS - 1, 1, False)
            act.wait_ge(sums_stored, 16 * OUTS)

        @block.gpsimd
        def _(pool):
            nc.gpsimd.memset(ones[:, :], 0.0).then_inc(ones_zeroed, 1)
            pool.wait_ge(ones_zeroed, 1)
            nc.gpsimd.memset(ones[0:E, 32:33], 1.0).then_inc(ones_ready, 1)
            nc.gpsimd.memset(ones[E:2 * E, 33:34], 1.0).then_inc(ones_ready, 1)
            pool.wait_ge(ones_ready, 2)

            def stacks(i, j, odd):
                src = slice(E * odd, E * odd + E)
                for n, k in enumerate((j, ITERS + i)):
                    for h in range(2):
                        at = (2 * odd + n) * BATCH + h * HB
                        pool.wait_ge(xtmp_ready, 8 * i + 4 * odd + 2 * n + h + 1)
                        nc.gpsimd.tensor_tensor(stack[src, at:at + HB], xq[src, k, h * HB:(h + 1) * HB],
                                                stack[src, at:at + HB].bitcast(f32),
                                                ALU.subtract).then_inc(xlo_ready, 1)

            def pool_round(i):
                j = row_of(pool, i)
                stacks(i, j, 0)
                for b in range(BLOCKS):
                    n = b % KRING
                    pool.wait_ge(khi_ready, BLOCKS * i + b + 1)
                    nc.gpsimd.tensor_tensor(klo[:, n, :], kraw[:, n, :], khi[:, n, :].bitcast(f32),
                                            ALU.subtract).then_inc(klo_ready, 1)
                    if b == KRING - 1:
                        pool.wait_ge(klo_ready, BLOCKS * i + b + 1)
                        stacks(i, j, 1)
                        pool.wait_ge(xlo_ready, 8 * i + 8)

            with pool.Fori(0, ITERS) as i:
                pool_round(i)

        @block.tensor
        def _(pe):
            def rhs(odd, place, j, c):
                base = 2 * odd * BATCH + c * CH
                at = base + second_row(place, j) * BATCH
                return stack[:, at:at + CH] if isinstance(at, int) else stack[:, bass.ds(at, CH)]

            def half(i, j, tile, h, first):
                local = 2 * tile + h
                back, user = before(local, TBUF)
                if not (first and back):
                    pe.wait_ge(prod_ready, HALVES * (i - back) + user + 1)
                s = slot_of(tile)
                if tile == SINGLE:
                    terms = [(s, lambda c: stack[:, 2 * BATCH + c * CH:2 * BATCH + (c + 1) * CH]),
                             (s + 1, lambda c: stack[:, BATCH + c * CH:BATCH + (c + 1) * CH])]
                else:
                    odd = int(tile > SINGLE)
                    place = tile - (SINGLE + 1) * odd
                    terms = [(s, lambda c: rhs(odd, place, j, c))]
                steps = [(part, slot, x_of) for slot, x_of in terms for part in (khi, klo)]
                for m, (part, slot, x_of) in enumerate(steps):
                    at = slot % BLK * 128
                    for c in range(2):
                        last = nc.tensor.matmul(tps[:, local % TBUF, c * CH:(c + 1) * CH],
                                                part[:, slot // BLK % KRING, at:at + 128], x_of(2 * h + c),
                                                start=m == 0, stop=m == len(steps) - 1)
                last.then_inc(t_ready, 1)

            def products(i, j, tile, first):
                s = slot_of(tile)
                if s % BLK == 0 or tile == SINGLE:
                    b = (s + (tile == SINGLE)) // BLK
                    pe.wait_ge(klo_ready, BLOCKS * i + b + 1)
                stacks_needed = {0: 1, ITERS: 2, SINGLE: 3, SINGLE + 1 + ITERS: 4}.get(tile)
                if stacks_needed:
                    pe.wait_ge(xhi_ready, 8 * i + 2 * stacks_needed)
                    pe.wait_ge(xlo_ready, 8 * i + 2 * stacks_needed)
                for h in range(2):
                    half(i, j, tile, h, first)

            def sum_tile(i, tile, first):
                odd = int(tile > SINGLE)
                place = tile - GROUP * odd
                if place == 0 and not first:
                    pe.wait_ge(sums_copied, 2 * i - 1 + odd)
                pe.wait_ge(prod_ready, HALVES * i + 2 * tile + 2)
                end = GROUP - 1 - odd
                for c in range(CHUNKS):
                    last = nc.tensor.matmul(rps[32 * c:32 * c + 32, odd, :],
                                            ones[:, 32 - 2 * place:64 - 2 * place],
                                            prod[:, (2 * tile + c // 2) % PBUF, c % 2 * CH:(c % 2 + 1) * CH],
                                            start=place == 0, stop=place == end)
                last.then_inc(tile_summed, 1)

            pe.wait_ge(ones_ready, 2)
            for tile in range(TILES):
                products(0, ITERS - 1, tile, True)
                if tile:
                    sum_tile(0, tile - 1, True)
            with pe.Fori(1, ITERS) as i:
                j = row_of(pe, i)
                products(i, j, 0, False)
                sum_tile(i - 1, TILES - 1, False)
                for tile in range(1, TILES):
                    products(i, j, tile, False)
                    sum_tile(i, tile - 1, False)
            sum_tile(ITERS - 1, TILES - 1, False)

        @block.vector
        def _(dve):
            def multiply(i, j, tile, first):
                for h in range(2):
                    local = 2 * tile + h
                    back, user = before(local, PBUF)
                    if not (first and back):
                        dve.wait_ge(tile_summed, TILES * (i - back) + user // 2 + 1)
                    dve.wait_ge(t_ready, HALVES * i + local + 1)
                    b = slice(h * HB, (h + 1) * HB)
                    if tile == SINGLE:
                        for rows, k in ((slice(0, E), j), (slice(E, 2 * E), ITERS + i)):
                            last = nc.vector.tensor_tensor(prod[rows, local % PBUF, :],
                                                           tps[rows, local % TBUF, :], xq[rows, k, b], ALU.mult)
                    else:
                        place = tile if tile < SINGLE else tile - SINGLE - 1
                        second = second_row(place, j)
                        k = j + (place + 1) if isinstance(second, int) and not second else \
                            (j * (second * -1 + 1) + (place + 1)) % XT
                        last = nc.vector.tensor_tensor(prod[:, local % PBUF, :], tps[:, local % TBUF, :],
                                                       xq[:, k, b], ALU.mult)
                    last.then_inc(prod_ready, 1)

            for tile in range(TILES):
                if tile < len(first_x) - 1:
                    dve.wait_ge(x_loaded[first_x[tile + 1]], 16)
                if tile == 0:
                    dve.wait_ge(x_loaded[first_x[0]], 16)
                multiply(0, ITERS - 1, tile, True)
            dve.wait_ge(x_rest_loaded, 16 * len(later_x))
            with dve.Fori(1, ITERS) as i:
                j = row_of(dve, i)
                for tile in range(TILES):
                    multiply(i, j, tile, False)


def tiles_of_round(i):
    j = ITERS - 1 - i
    even = [(2 * j, k) for k in range(j + 1, XT)] + [(FIELDS - 2 - 2 * j, k) for k in range(XT - j, XT)]
    return even, [(r + 1, k) for r, k in even]


def pair_number(r, c):
    return r * FIELDS - r * (r + 1) // 2 + c - r - 1


def kernel(r_x, L0_rec_kernel):
    import numpy as np
    import concourse.bacc as bacc
    from concourse.bass_utils import run_bass_kernel_spmd

    x = np.asarray(r_x)
    wk = np.asarray(L0_rec_kernel)
    xt = np.ascontiguousarray(x.transpose(1, 2, 0)).reshape(XT, 2 * E, BATCH)
    by_in = wk.transpose(2, 1, 0)
    by_out = wk.transpose(0, 1, 2)
    wt = np.zeros((ITERS, E, SLOTS, 2, E), wk.dtype)
    order = np.zeros((OUTS, GROUP, 2), np.int64) - 1
    for i in range(ITERS):
        j = ITERS - 1 - i
        for odd, tiles in enumerate(tiles_of_round(i)):
            first = odd * (SINGLE + 2)
            for s, (r, k) in enumerate(tiles):
                for m in range(2):
                    n = pair_number(r, 2 * k + m)
                    wt[i, :, first + s, m] = by_in[:, n]
                    order[2 * i + odd, s, m] = n
        top, low = pair_number(2 * j, 2 * j + 1), pair_number(FIELDS - 2 - 2 * j, FIELDS - 1 - 2 * j)
        wt[i, :, SINGLE, 0] = by_out[:, top]
        wt[i, :, SINGLE + 1, 1] = by_in[:, low]
        order[2 * i, SINGLE] = top, low
    wt = np.ascontiguousarray(wt.reshape(ITERS, E, BLOCKS, BLK * 128).transpose(0, 2, 1, 3))

    f32 = mybir.dt.float32
    nc = bacc.Bacc("TRN2", target_bir_lowering=False, num_devices=1)
    args = [nc.dram_tensor("x_t", xt.shape, f32, kind="ExternalInput").ap(),
            nc.dram_tensor("w_t", wt.shape, f32, kind="ExternalInput").ap(),
            nc.dram_tensor("sums_t", (OUTS, 128, CH), f32, kind="ExternalOutput").ap()]
    build(nc, *args)
    got = run_bass_kernel_spmd(nc, [{"x_t": xt, "w_t": wt}], core_ids=[0]).results[0]["sums_t"]
    got = np.asarray(got).reshape(OUTS, CHUNKS, 2 * GROUP, CH).transpose(1, 3, 0, 2).reshape(BATCH, -1)
    order = order.reshape(-1)
    place = np.empty(PAIRS, np.int64)
    place[order[order >= 0]] = np.nonzero(order >= 0)[0]
    return np.ascontiguousarray(got[:, place])
```

```python
from contextlib import ExitStack

import concourse.bass as bass
from concourse import mybir

BATCH = 2048
FIELDS = 32
E = 64
PAIRS = FIELDS * (FIELDS - 1) // 2
NAT = 4
XT = (FIELDS - NAT) // 2
ROUNDS = XT // 2
SINGLE = XT - 1
TILES = 2 * SINGLE + 1
PLACES = SINGLE
CH = 512
CHUNKS = BATCH // CH
HB = BATCH // 2
BT = BATCH // 128
RW = NAT * E
PIECES = 4
PB = BT // PIECES
CORNER = NAT - 1
BLK = 4 * 128
KRING = 3
TBUF, PBUF = 3, 5
GROUP = SINGLE + 1
SUM_LAG = 2
ROW_LAG = 4


def steps(rows_after, tiles):
    out = []
    for t in tiles:
        out.append(("tile", t))
        out += [("row", r) for r, after in rows_after.items() if t in after]
    return out


EVEN_STEPS = steps({0: (0, 1, 3, 4), 1: (6, 7, 9, 10)}, range(0, SINGLE + 1))
ODD_STEPS = steps({2: (15, 16, 18, 19), 3: (21, 22, 23, 24)}, range(SINGLE + 1, TILES))

UNITS = []
for kind, n in EVEN_STEPS + ODD_STEPS:
    if kind == "tile":
        UNITS += [("tile", n, 0), ("tile", n, 1)]
    else:
        UNITS.append(("row", n, sum(u[:2] == ("row", n) for u in UNITS)))
NU = len(UNITS)
ROW_UNITS = [l for l, u in enumerate(UNITS) if u[0] == "row"]
CORNER_UNITS = CORNER * PIECES
T_OF = [l % TBUF for l in range(NU)]
if NU % TBUF == 1:
    T_OF[-1] = 1
P_OF = [l % PBUF for l in range(NU)]

SLOTS = [("row", 0), ("row", 0), 0, 1, 2, 3, 4, 5, ("row", 1), ("row", 1), 6, 7, 8, 9, 10, 11,
         12, SINGLE, SINGLE, 14, ("row", 2), ("row", 2), 15, 16, 17, 18, 19, 20,
         ("row", 3), ("row", 3), 21, 22, 23, 24, 25, 26]
BLOCKS = len(SLOTS) // 4


def slot_of(tile):
    return SLOTS.index(tile)


def last_unit_of_block(b):
    readers = SLOTS[4 * b:4 * b + 4]
    return max(l for l, u in enumerate(UNITS) if (u[:2] if u[0] == "row" else u[1]) in readers)


def last_unit_of_tile(tile):
    return UNITS.index(("tile", tile, 1))


def user_before(l, buffers):
    for back, units in ((0, range(l - 1, -1, -1)), (1, range(NU - 1, l, -1))):
        for m in units:
            if buffers[m] == buffers[l]:
                return back, m


def second_row(place, j):
    most = j if isinstance(j, int) else ROUNDS - 2
    return 0 if place + most < PLACES else (j + (place + 16 - PLACES)) // 16


def build(nc, x, xn, w, wc, out, out_rows):
    f32, f32r = mybir.dt.float32, mybir.dt.float32r
    ALU, ACT, AX = mybir.AluOpType, mybir.ActivationFunctionType, mybir.AxisListType

    ctx = ExitStack()
    with ctx:
        def sb(name, shape, dt=f32):
            return ctx.enter_context(nc.sbuf_tensor(name, shape, dt))

        def sem(name):
            return ctx.enter_context(nc.semaphore(name))

        xs = sb("xs", [128, XT + 2, BATCH])
        xnat = xs[:, XT:XT + 2, :].rearrange("p a b -> p (a b)").rearrange("p (t n) -> p t n", n=RW)
        stack = sb("stack", [128, 4 * BATCH], f32r)
        kraw = sb("kraw", [128, KRING, BLK])
        khi = sb("khi", [128, KRING, BLK], f32r)
        klo = sb("klo", [128, KRING, BLK], f32r)
        prod = sb("prod", [128, PBUF, HB])
        sums = sb("sums", [128, 2, CH])
        row_sums = sb("row_sums", [128, 2, BT, 2, NAT])
        ones = sb("ones", [128, 64])
        tps = ctx.enter_context(nc.psum_tensor("tps", [128, TBUF, HB], f32))
        rps = ctx.enter_context(nc.psum_tensor("rps", [128, 2, CH], f32))

        first_x = list(range(ROUNDS - 1, XT))
        corner_loaded = [sem("corner_a_half_loaded"), sem("corner_a_loaded"), sem("corner_b_loaded")]
        xnat_loaded = sem("xnat_loaded")
        x_loaded = {k: sem(f"x_loaded_{k}") for k in first_x}
        x_rest_loaded = sem("x_rest_loaded")
        kraw_loaded = [sem(f"kraw_loaded_{n}") for n in range(KRING)]
        ones_zeroed = sem("ones_zeroed")
        ones_ready = sem("ones_ready")
        khi_ready = sem("khi_ready")
        klo_ready = sem("klo_ready")
        xtmp_ready = sem("xtmp_ready")
        xhi_ready = sem("xhi_ready")
        xlo_ready = sem("xlo_ready")
        t_ready = sem("t_ready")
        prod_ready = sem("prod_ready")
        tile_summed = sem("tile_summed")
        halves_added = sem("halves_added")
        row_reduced = sem("row_reduced")
        sums_copied = sem("sums_copied")
        sums_stored = sem("sums_stored")
        rows_stored = [sem("even_rows_stored"), sem("odd_rows_stored")]

        def units_before(i):
            return NU * i + CORNER_UNITS

        def blocks_before(i):
            return BLOCKS * i + CORNER

        def halves_before(i):
            return 8 * i + 2 * CORNER

        def pieces_before(i):
            return 4 * PIECES * i + CORNER_UNITS

        def row_of(engine, i):
            return ROUNDS - 1 - i if isinstance(i, int) else engine.snap(i * -1 + (ROUNDS - 1))

        block = ctx.enter_context(nc.Block())

        @block.sync
        def _(sp):
            def load_corner(n):
                for top in (0, E):
                    sp.dma_start(kraw[top:top + E, n, :RW], wc[n]).then_inc(kraw_loaded[n], 16)

            def load_block(i, b, first):
                n = b % KRING
                sp.wait_ge(klo_ready, blocks_before(i) + b - KRING + 1)
                for top in (0, E):
                    sp.dma_start(kraw[top:top + E, n, :], w[i, b]).then_inc(kraw_loaded[n], 16)

            def load_x(k):
                sp.dma_start(xs[:, k, :], x[k]).then_inc(x_loaded[k], 16)

            load_corner(0)
            sp.dma_start(xs[:, 0, :HB], x[XT, :, :HB]).then_inc(corner_loaded[0], 16)
            sp.dma_start(xs[:, 0, HB:], x[XT, :, HB:]).then_inc(corner_loaded[1], 16)
            load_corner(1)
            sp.dma_start(xnat, xn).then_inc(xnat_loaded, 16)
            sp.dma_start(xs[0:E, 1, :], x[XT + 1, 0:E, :]).then_inc(corner_loaded[2], 16)
            load_corner(2)
            for k in first_x[:2]:
                load_x(k)
            for b in range(BLOCKS):
                load_block(0, b, True)
                if b < KRING:
                    for k in first_x[2 + 2 * b:4 + 2 * b]:
                        load_x(k)
                if b == KRING:
                    sp.wait_ge(xlo_ready, halves_before(0))
                    for k in range(ROUNDS - 2, -1, -1):
                        sp.dma_start(xs[:, k, :], x[k]).then_inc(x_rest_loaded, 16)
            with sp.Fori(1, ROUNDS) as i:
                for b in range(BLOCKS):
                    load_block(i, b, False)

        @block.scalar
        def _(act):
            def split_half(k, odd, slot, h):
                src = slice(E * odd, E * odd + E)
                dst = slice(E * (1 - odd), E * (1 - odd) + E)
                at = slot * BATCH + h * HB
                source = xs[src, k, h * HB:(h + 1) * HB]
                nc.scalar.activation(stack[src, at:at + HB], source, ACT.Copy).then_inc(xtmp_ready, 1)
                nc.scalar.activation(stack[dst, at:at + HB], source, ACT.Copy).then_inc(xhi_ready, 1)

            def even_half(i, j, n, h, first):
                if h == 0:
                    if first:
                        act.wait_ge(t_ready, PIECES if n == 0 else CORNER_UNITS)
                        act.wait_ge(x_loaded[ROUNDS + i if n else j], 16)
                    else:
                        act.wait_ge(t_ready, units_before(i - 1) + last_unit_of_tile(SINGLE - 1 + n) + 1)
                split_half(ROUNDS + i if n else j, 0, n, h)

            def odd_half(i, j, n, h):
                if h == 0:
                    act.wait_ge(t_ready, units_before(i))
                split_half(ROUNDS + i if n else j, 1, 2 + n, h)

            def weights(i, b, back=0):
                n = b % KRING
                act.wait_ge(kraw_loaded[n], 32 * (KRING * i + b // KRING + 2))
                if back == "corner":
                    act.wait_ge(t_ready, (b + 1) * PIECES)
                else:
                    act.wait_ge(t_ready, units_before(i - back) + last_unit_of_block((b - KRING) % BLOCKS) + 1)
                nc.scalar.activation(khi[:, n, :], kraw[:, n, :], ACT.Copy).then_inc(khi_ready, 1)

            def store_rows(i, odd):
                act.wait_ge(row_reduced, pieces_before(i) + 2 * PIECES * (odd + 1))
                act.dma_start(out_rows[i, odd], row_sums[:, odd]).then_inc(rows_stored[odd], 16)

            def store_sums(i, odd, first):
                act.wait_ge(tile_summed, TILES * i + (TILES if odd else GROUP))
                if not first:
                    act.wait_ge(sums_stored, 16 * (2 * i + odd))
                nc.scalar.activation(sums[:, odd, :], rps[:, odd, :], ACT.Copy).then_inc(sums_copied, 1)
                act.wait_ge(sums_copied, 2 * i + odd + 1)
                act.dma_start(out[2 * i + odd], sums[:, odd, :]).then_inc(sums_stored, 16)

            def corner():
                for n in range(CORNER):
                    act.wait_ge(kraw_loaded[n], 32)
                    nc.scalar.activation(khi[:, n, :RW], kraw[:, n, :RW], ACT.Copy).then_inc(khi_ready, 1)
                    for h in range(2):
                        act.wait_ge(corner_loaded[2 if n == 2 else max(n, h)], 16)
                        split_half(n // 2, n % 2, (0, 2, 1)[n], h)

            def even_part(i, j, first):
                weights(i, 2, "corner" if first else 1)
                odd_half(i, j, 0, 0)
                if not first:
                    store_sums(i - 1, 1, False)
                    store_rows(i - 1, 1)
                weights(i, 3)
                odd_half(i, j, 0, 1)
                weights(i, 4)
                odd_half(i, j, 1, 0)
                odd_half(i, j, 1, 1)
                weights(i, 5)

            def odd_part(i, following, j, last, first=False):
                weights(i, 6)
                if not last:
                    even_half(following, j, 0, 0, False)
                store_sums(i, 0, first)
                store_rows(i, 0)
                if not last:
                    even_half(following, j, 0, 1, False)
                weights(i, 7)
                weights(i, 8)
                if not last:
                    even_half(following, j, 1, 0, False)
                    even_half(following, j, 1, 1, False)
                    weights(following, 0, 1)
                    weights(following, 1, 1)

            corner()
            for h in range(2):
                even_half(0, ROUNDS - 1, 0, h, True)
            weights(0, 0, "corner")
            weights(0, 1, "corner")
            for h in range(2):
                even_half(0, ROUNDS - 1, 1, h, True)
            act.wait_ge(row_reduced, CORNER_UNITS)
            act.dma_start(out_rows[ROUNDS, 0], row_sums[:, 0]).then_inc(rows_stored[0], 16)
            act.dma_start(out_rows[ROUNDS, 1, :, :, 0, :], row_sums[:, 1, :, 0, :]).then_inc(rows_stored[1], 16)
            even_part(0, ROUNDS - 1, True)
            act.wait_ge(x_rest_loaded, 16 * (ROUNDS - 1))
            odd_part(0, 1, ROUNDS - 2, False, True)
            even_part(1, ROUNDS - 2, False)
            with act.Fori(2, ROUNDS) as i:
                j = row_of(act, i)
                odd_part(i - 1, i, j, False)
                even_part(i, j, False)
            odd_part(ROUNDS - 1, ROUNDS, None, True)
            store_sums(ROUNDS - 1, 1, False)
            store_rows(ROUNDS - 1, 1)
            act.wait_ge(sums_stored, 16 * 2 * ROUNDS)
            for odd in range(2):
                act.wait_ge(rows_stored[odd], 16 * (ROUNDS + 1))

        @block.gpsimd
        def _(pool):
            nc.gpsimd.memset(ones[:, :], 0.0).then_inc(ones_zeroed, 1)
            pool.wait_ge(ones_zeroed, 1)
            nc.gpsimd.memset(ones[0:E, 32:33], 1.0).then_inc(ones_ready, 1)
            nc.gpsimd.memset(ones[E:2 * E, 33:34], 1.0).then_inc(ones_ready, 1)
            pool.wait_ge(ones_ready, 2)

            def low_half(k, odd, slot, h, nth):
                src = slice(E * odd, E * odd + E)
                at = slot * BATCH + h * HB
                pool.wait_ge(xtmp_ready, nth)
                nc.gpsimd.tensor_tensor(stack[src, at:at + HB], xs[src, k, h * HB:(h + 1) * HB],
                                        stack[src, at:at + HB].bitcast(f32), ALU.subtract).then_inc(xlo_ready, 1)

            def even_half(i, j, n, h):
                low_half(ROUNDS + i if n else j, 0, n, h, halves_before(i) + 2 * n + h + 1)

            def odd_half(i, j, n, h, blocks, pieces):
                pool.wait_ge(klo_ready, blocks)
                pool.wait_ge(halves_added, 2 * pieces)
                low_half(ROUNDS + i if n else j, 1, 2 + n, h, halves_before(i) + 4 + 2 * n + h + 1)
                pool.wait_ge(xlo_ready, halves_before(i) + 4 + 2 * n + h + 1)

            def weights(i, b, cols=BLK, nth=None):
                n = b % KRING
                pool.wait_ge(khi_ready, blocks_before(i) + b + 1 if nth is None else nth)
                nc.gpsimd.tensor_tensor(klo[:, n, :cols], kraw[:, n, :cols], khi[:, n, :cols].bitcast(f32),
                                        ALU.subtract).then_inc(klo_ready, 1)

            def add_halves(buf, unit, piece):
                v = prod[:, buf, :].rearrange("p (n o) -> p n o", o=E)
                pool.wait_ge(prod_ready, unit)
                for m, width in enumerate((E // 2, E // 4)):
                    if m:
                        pool.wait_ge(halves_added, 2 * piece - 1)
                    nc.gpsimd.tensor_tensor(v[:, :, 0:width], v[:, :, 0:width], v[:, :, width:2 * width],
                                            ALU.add).then_inc(halves_added, 1)

            def piece(i, n):
                l = ROW_UNITS[n]
                add_halves(P_OF[l], units_before(i) + l + 1, pieces_before(i) + n + 1)

            def even_part(i, j):
                blocks, pieces = blocks_before(i), pieces_before(i)
                weights(i, 2)
                piece(i, 0)
                piece(i, 1)
                odd_half(i, j, 0, 0, blocks + 3, pieces + 2)
                piece(i, 2)
                piece(i, 3)
                weights(i, 3)
                odd_half(i, j, 0, 1, blocks + 4, pieces + 4)
                piece(i, 4)
                weights(i, 4)
                piece(i, 5)
                odd_half(i, j, 1, 0, blocks + 5, pieces + 6)
                piece(i, 6)
                piece(i, 7)
                odd_half(i, j, 1, 1, blocks + 5, pieces + 8)
                weights(i, 5)

            def odd_part(i, following, j, last):
                weights(i, 6)
                if not last:
                    even_half(following, j, 0, 0)
                piece(i, 8)
                piece(i, 9)
                if not last:
                    even_half(following, j, 0, 1)
                piece(i, 10)
                weights(i, 7)
                piece(i, 11)
                weights(i, 8)
                if not last:
                    even_half(following, j, 1, 0)
                piece(i, 12)
                piece(i, 13)
                if not last:
                    even_half(following, j, 1, 1)
                    weights(following, 0)
                piece(i, 14)
                piece(i, 15)
                if not last:
                    weights(following, 1)

            def corner_piece(n):
                add_halves(n % PBUF, n + 1, n + 1)

            def corner_odd_half(h, pieces):
                pool.wait_ge(klo_ready, 2)
                if pieces:
                    pool.wait_ge(halves_added, 2 * pieces)
                low_half(0, 1, 2, h, 3 + h)
                pool.wait_ge(xlo_ready, 3 + h)

            weights(0, 0, RW, 1)
            low_half(0, 0, 0, 0, 1)
            low_half(0, 0, 0, 1, 2)
            weights(0, 1, RW, 2)
            corner_piece(0)
            corner_odd_half(0, 1)
            corner_piece(1)
            corner_odd_half(1, 2)
            corner_piece(2)
            weights(0, 2, RW, 3)
            corner_piece(3)
            low_half(1, 0, 1, 0, 5)
            corner_piece(4)
            low_half(1, 0, 1, 1, 6)
            corner_piece(5)
            even_half(0, ROUNDS - 1, 0, 0)
            corner_piece(6)
            even_half(0, ROUNDS - 1, 0, 1)
            corner_piece(7)
            weights(0, 0)
            corner_piece(8)
            weights(0, 1)
            corner_piece(9)
            corner_piece(10)
            corner_piece(11)
            even_half(0, ROUNDS - 1, 1, 0)
            even_half(0, ROUNDS - 1, 1, 1)
            even_part(0, ROUNDS - 1)
            with pool.Fori(1, ROUNDS) as i:
                j = row_of(pool, i)
                odd_part(i - 1, i, j, False)
                even_part(i, j)
            odd_part(ROUNDS - 1, ROUNDS, None, True)

        @block.tensor
        def _(pe):
            def x_parts(odd, place, j, c):
                at = 2 * odd * BATCH + c * CH + second_row(place, j) * BATCH
                return stack[:, at:at + CH] if isinstance(at, int) else stack[:, bass.ds(at, CH)]

            def tile_half(j, tile, h, buf):
                if tile == SINGLE:
                    terms = [(slot_of(tile), lambda c: stack[:, 2 * BATCH + c * CH:2 * BATCH + (c + 1) * CH]),
                             (slot_of(tile) + 1, lambda c: stack[:, BATCH + c * CH:BATCH + (c + 1) * CH])]
                else:
                    odd = int(tile > SINGLE)
                    terms = [(slot_of(tile), lambda c: x_parts(odd, tile - (SINGLE + 1) * odd, j, c))]
                passes = [(part, slot, x_of) for slot, x_of in terms for part in (khi, klo)]
                for m, (part, slot, x_of) in enumerate(passes):
                    at = slot % 4 * 128
                    for c in range(2):
                        last = nc.tensor.matmul(tps[:, buf, c * CH:(c + 1) * CH],
                                                part[:, slot // 4 % KRING, at:at + 128], x_of(2 * h + c),
                                                start=m == 0, stop=m == len(passes) - 1)
                return last

            def row_piece(stack_slot, ring, at, piece, buf):
                for t in range(PB):
                    first = stack_slot * BATCH + (piece * PB + t) * 128
                    for part in (khi, klo):
                        last = nc.tensor.matmul(tps[:, buf, t * RW:(t + 1) * RW], stack[:, first:first + 128],
                                                part[:, ring, at:at + RW], start=part is khi, stop=part is klo)
                return last

            def unit(i, j, l, first):
                kind, n, h = UNITS[l]
                back, user = user_before(l, T_OF)
                pe.wait_ge(prod_ready, units_before(i) if first and back else units_before(i - back) + user + 1)
                slot = slot_of(n) if kind == "tile" else SLOTS.index(("row", n))
                if h == 0:
                    last_slot = slot + (n == SINGLE and kind == "tile")
                    pe.wait_ge(klo_ready, blocks_before(i) + last_slot // 4 + 1)
                half = h if kind == "tile" else h * 2 // PIECES
                need = None
                if kind == "row":
                    need = n
                elif n in (0, SINGLE, SINGLE + 1):
                    need = {0: 0, SINGLE: 2, SINGLE + 1: 2}[n]
                elif (n - (SINGLE + 1) * (n > SINGLE)) + ROUNDS - 1 >= PLACES:
                    need = 1 + 2 * (n > SINGLE)
                if need is not None:
                    pe.wait_ge(xhi_ready, halves_before(i) + 2 * need + half + 1)
                    pe.wait_ge(xlo_ready, halves_before(i) + 2 * need + half + 1)
                if kind == "tile":
                    last = tile_half(j, n, h, T_OF[l])
                else:
                    last = row_piece(n, slot // 4 % KRING, 0, h, T_OF[l])
                last.then_inc(t_ready, 1)

            def sum_tile(i, tile, first):
                odd = int(tile > SINGLE)
                place = tile - GROUP * odd
                if place == 0 and not first:
                    pe.wait_ge(sums_copied, 2 * i - 1 + odd)
                l = last_unit_of_tile(tile)
                pe.wait_ge(prod_ready, units_before(i) + l + 1)
                for c in range(CHUNKS):
                    last = nc.tensor.matmul(rps[32 * c:32 * c + 32, odd, :],
                                            ones[:, 32 - 2 * place:64 - 2 * place],
                                            prod[:, P_OF[l - 1 + c // 2], c % 2 * CH:(c % 2 + 1) * CH],
                                            start=place == 0, stop=place == GROUP - 1 - odd)
                last.then_inc(tile_summed, 1)

            def round_(i, j, first):
                for l in range(NU):
                    unit(i, j, l, first)
                    due = l - SUM_LAG
                    if due >= 0 and UNITS[due][0] == "tile" and UNITS[due][2]:
                        sum_tile(i, UNITS[due][1], first)
                    if due < 0 and not first and UNITS[due][0] == "tile" and UNITS[due][2]:
                        sum_tile(i - 1, UNITS[due][1], False)

            for n in range(CORNER_UNITS):
                row, piece = n // PIECES, n % PIECES
                if n >= TBUF:
                    pe.wait_ge(prod_ready, n - TBUF + 1)
                pe.wait_ge(klo_ready, row + 1)
                pe.wait_ge(xhi_ready, 2 * row + piece * 2 // PIECES + 1)
                pe.wait_ge(xlo_ready, 2 * row + piece * 2 // PIECES + 1)
                row_piece((0, 2, 1)[row], row, 0, piece, n % TBUF).then_inc(t_ready, 1)
            pe.wait_ge(ones_ready, 2)
            round_(0, ROUNDS - 1, True)
            with pe.Fori(1, ROUNDS) as i:
                j = row_of(pe, i)
                round_(i, j, False)
            sum_tile(ROUNDS - 1, TILES - 1, False)

        @block.vector
        def _(dve):
            def reduce_row(buf, half, place, piece, nth):
                dve.wait_ge(halves_added, 2 * nth)
                terms = prod[:, buf, :].rearrange("p (t c o) -> p t c o", c=NAT, o=E)[:, :, :, 0:E // 4]
                nc.vector.tensor_reduce(row_sums[:, half, piece * PB:(piece + 1) * PB, place, :], terms,
                                        AX.X, ALU.add).then_inc(row_reduced, 1)

            def multiply_row(piece, tbuf, pbuf):
                last_fields = xnat[:, piece * PB:(piece + 1) * PB, :].rearrange("p t n -> p (t n)")
                nc.vector.tensor_tensor(prod[:, pbuf, :], tps[:, tbuf, :], last_fields,
                                        ALU.mult).then_inc(prod_ready, 1)

            def multiply_half(i, j, tile, h, tbuf, pbuf):
                b = slice(h * HB, (h + 1) * HB)
                if tile == SINGLE:
                    for rows, k in ((slice(0, E), j), (slice(E, 2 * E), ROUNDS + i)):
                        last = nc.vector.tensor_tensor(prod[rows, pbuf, :], tps[rows, tbuf, :],
                                                       xs[rows, k, b], ALU.mult)
                else:
                    place = tile if tile < SINGLE else tile - SINGLE - 1
                    second = second_row(place, j)
                    k = j + (place + 1) if isinstance(second, int) and not second else \
                        (j * (second * -1 + 1) + (place + 1)) % (XT + 2)
                    last = nc.vector.tensor_tensor(prod[:, pbuf, :], tps[:, tbuf, :], xs[:, k, b], ALU.mult)
                last.then_inc(prod_ready, 1)

            def unit(i, j, l, first):
                kind, n, h = UNITS[l]
                back, user = user_before(l, P_OF)
                if not (first and back):
                    if UNITS[user][0] == "tile":
                        dve.wait_ge(tile_summed, TILES * (i - back) + UNITS[user][1] + 1)
                    else:
                        dve.wait_ge(row_reduced, pieces_before(i - back) + ROW_UNITS.index(user) + 1)
                dve.wait_ge(t_ready, units_before(i) + l + 1)
                if kind == "tile":
                    multiply_half(i, j, n, h, T_OF[l], P_OF[l])
                else:
                    multiply_row(h, T_OF[l], P_OF[l])

            def reduce_due(i, l):
                due = l - ROW_LAG
                if due in ROW_UNITS:
                    _, row, piece = UNITS[due]
                    n = ROW_UNITS.index(due)
                    if n in (0, 2 * PIECES):
                        dve.wait_ge(rows_stored[row // 2], 16 * (i + 1))
                    reduce_row(P_OF[due], row // 2, row % 2, piece, pieces_before(i) + n + 1)

            def round_(i, j, first):
                for l in range(NU):
                    reduce_due(i, l)
                    if first and UNITS[l][0] == "tile" and UNITS[l][2] == 0 and UNITS[l][1] + 1 < len(first_x):
                        dve.wait_ge(x_loaded[first_x[UNITS[l][1] + 1]], 16)
                    unit(i, j, l, first)

            dve.wait_ge(xnat_loaded, 16)
            for n in range(CORNER_UNITS + ROW_LAG):
                due = n - ROW_LAG
                if due >= 0:
                    row = due // PIECES
                    reduce_row(due % PBUF, row // 2, row % 2, due % PIECES, due + 1)
                if n < CORNER_UNITS:
                    if n >= PBUF:
                        dve.wait_ge(row_reduced, n - PBUF + 1)
                    dve.wait_ge(t_ready, n + 1)
                    multiply_row(n % PIECES, n % TBUF, n % PBUF)
            dve.wait_ge(row_reduced, CORNER_UNITS)
            dve.wait_ge(x_loaded[first_x[0]], 16)
            round_(0, ROUNDS - 1, True)
            dve.wait_ge(x_rest_loaded, 16 * (ROUNDS - 1))
            with dve.Fori(1, ROUNDS) as i:
                j = row_of(dve, i)
                round_(i, j, False)


def tiles_of_round(i):
    j = ROUNDS - 1 - i
    even = [(2 * j, k) for k in range(j + 1, XT)] + [(2 * (XT - 1 - j), k) for k in range(XT - j, XT)]
    return even, [(r + 1, k) for r, k in even]


def rows_of_round(i):
    j = ROUNDS - 1 - i
    return 2 * j, 2 * (XT - 1 - j), 2 * j + 1, 2 * (XT - 1 - j) + 1


def pair_number(r, c):
    return r * FIELDS - r * (r + 1) // 2 + c - r - 1


def kernel(r_x, L0_rec_kernel):
    import numpy as np
    import concourse.bacc as bacc
    from concourse.bass_utils import run_bass_kernel_spmd

    x = np.asarray(r_x)
    wk = np.asarray(L0_rec_kernel)
    xt = np.ascontiguousarray(x.transpose(1, 2, 0)).reshape(FIELDS // 2, 2 * E, BATCH)
    xn = np.ascontiguousarray(x[:, FIELDS - NAT:].reshape(BT, 128, RW).transpose(1, 0, 2))
    by_in = wk.transpose(2, 1, 0)
    by_out = wk.transpose(0, 1, 2)
    wt = np.zeros((ROUNDS, E, 4 * BLOCKS, 2, E), wk.dtype)
    wc = np.zeros((CORNER, E, NAT, E), wk.dtype)
    order = np.zeros((2 * ROUNDS, 16, 2), np.int64) - 1
    row_order = np.zeros((ROUNDS + 1, 2, 2, NAT), np.int64) - 1
    last_fields = range(FIELDS - NAT, FIELDS)
    for i in range(ROUNDS):
        j = ROUNDS - 1 - i
        for odd, tiles in enumerate(tiles_of_round(i)):
            for s, (r, k) in enumerate(tiles):
                for m in range(2):
                    n = pair_number(r, 2 * k + m)
                    wt[i, :, slot_of(s + (SINGLE + 1) * odd), m] = by_in[:, n]
                    order[2 * i + odd, s, m] = n
        top = pair_number(2 * j, 2 * j + 1)
        low = pair_number(2 * (XT - 1 - j), 2 * (XT - 1 - j) + 1)
        wt[i, :, slot_of(SINGLE), 0] = by_out[:, top]
        wt[i, :, slot_of(SINGLE) + 1, 1] = by_in[:, low]
        order[2 * i, SINGLE] = top, low
        for row, r in enumerate(rows_of_round(i)):
            for m, c in enumerate(last_fields):
                n = pair_number(r, c)
                wt[i, :, SLOTS.index(("row", row)) + m // 2, m % 2] = by_in[:, n]
                row_order[i, row // 2, row % 2, m] = n
    for row in range(CORNER):
        for m in range(row + 1, NAT):
            n = pair_number(FIELDS - NAT + row, FIELDS - NAT + m)
            wc[row, :, m] = by_in[:, n]
            row_order[ROUNDS, row // 2, row % 2, m] = n
    wt = np.ascontiguousarray(wt.reshape(ROUNDS, E, BLOCKS, BLK).transpose(0, 2, 1, 3))
    wc = wc.reshape(CORNER, E, RW)

    f32 = mybir.dt.float32
    nc = bacc.Bacc("TRN2", target_bir_lowering=False, num_devices=1)
    arrays = {"x_t": xt, "x_nat": xn, "w_t": wt, "w_corner": wc}
    args = [nc.dram_tensor(name, a.shape, f32, kind="ExternalInput").ap() for name, a in arrays.items()]
    args += [nc.dram_tensor("sums_t", (2 * ROUNDS, 128, CH), f32, kind="ExternalOutput").ap(),
             nc.dram_tensor("row_sums_t", (ROUNDS + 1, 2, 128, BT, 2, NAT), f32, kind="ExternalOutput").ap()]
    build(nc, *args)
    got = run_bass_kernel_spmd(nc, [arrays], core_ids=[0]).results[0]
    tiles = np.asarray(got["sums_t"]).reshape(2 * ROUNDS, CHUNKS, 32, CH).transpose(1, 3, 0, 2).reshape(BATCH, -1)
    rows = np.asarray(got["row_sums_t"]).transpose(3, 2, 0, 1, 4, 5).reshape(BATCH, -1)
    result = np.empty((BATCH, PAIRS), x.dtype)
    for source, where in ((tiles, order.reshape(-1)), (rows, row_order.reshape(-1))):
        result[:, where[where >= 0]] = source[:, where >= 0]
    return result
```

```python
from contextlib import ExitStack

import concourse.bass as bass
from concourse import mybir

BATCH = 2048
FIELDS = 32
E = 64
PAIRS = FIELDS * (FIELDS - 1) // 2
NAT = 4
XT = (FIELDS - NAT) // 2
ROUNDS = XT // 2
SINGLE = XT - 1
TILES = 2 * SINGLE + 1
PLACES = SINGLE
CH = 512
CHUNKS = BATCH // CH
HB = BATCH // 2
BT = BATCH // 128
RW = NAT * E
PIECES = 4
PB = BT // PIECES
CORNER_ROWS = 3
CORNER_TILES = 3
CORNER_UNITS = 2 * CORNER_TILES
BLK = 4 * 128
KRING = 3
TBUF, PBUF = 3, 7
GROUP = SINGLE + 1
SUM_LAG = 2
ROW_LAG = 4


PLACE_ORDER = [0] + [p for k in range(1, ROUNDS) for p in (k, ROUNDS - 1 + k)]
TILE_ORDER = PLACE_ORDER + [SINGLE] + [SINGLE + 1 + p for p in PLACE_ORDER]


def steps(rows_after, tiles, first):
    out = []
    for n, t in enumerate(tiles, first):
        out.append(("tile", t))
        out += [("row", r) for r, after in rows_after.items() if n in after]
    return out


EVEN_STEPS = steps({0: (0, 1, 3, 4), 1: (6, 7, 9, 10)}, TILE_ORDER[:SINGLE + 1], 0)
ODD_STEPS = steps({2: (14, 15, 17, 18), 3: (20, 21, 23, 24)}, TILE_ORDER[SINGLE + 1:], SINGLE + 1)

UNITS = []
for kind, n in EVEN_STEPS + ODD_STEPS:
    if kind == "tile":
        UNITS += [("tile", n, 0), ("tile", n, 1)]
    else:
        UNITS.append(("row", n, sum(u[:2] == ("row", n) for u in UNITS)))
NU = len(UNITS)
ROW_UNITS = [l for l, u in enumerate(UNITS) if u[0] == "row"]
assert NU % TBUF == 1
TURN = UNITS.index(("tile", SINGLE, 0))
T_OF = [l % TBUF if l < TURN else (l - 2) % TBUF if l == TURN else (l - 1) % TBUF for l in range(NU)]
P_OF = [l % PBUF for l in range(NU)]

SLOTS = [("row", 0), ("row", 0), *TILE_ORDER[:6], ("row", 1), ("row", 1), *TILE_ORDER[6:13],
         SINGLE, SINGLE, TILE_ORDER[14], ("row", 2), ("row", 2), *TILE_ORDER[15:21],
         ("row", 3), ("row", 3), *TILE_ORDER[21:]]
BLOCKS = len(SLOTS) // 4


def slot_of(tile):
    return SLOTS.index(tile)


def last_unit_of_block(b):
    readers = SLOTS[4 * b:4 * b + 4]
    return max(l for l, u in enumerate(UNITS) if (u[:2] if u[0] == "row" else u[1]) in readers)


def last_unit_of_tile(tile):
    return UNITS.index(("tile", tile, 1))


def user_before(l, buffers):
    for back, units in ((0, range(l - 1, -1, -1)), (1, range(NU - 1, l, -1))):
        for m in units:
            if buffers[m] == buffers[l]:
                return back, m


def second_row(place, j):
    most = j if isinstance(j, int) else ROUNDS - 2
    return 0 if place + most < PLACES else (j + (place + 16 - PLACES)) // 16


def build(nc, x, xn, w, wc, out, out_rows):
    f32, f32r = mybir.dt.float32, mybir.dt.float32r
    ALU, ACT, AX = mybir.AluOpType, mybir.ActivationFunctionType, mybir.AxisListType

    ctx = ExitStack()
    with ctx:
        def sb(name, shape, dt=f32):
            return ctx.enter_context(nc.sbuf_tensor(name, shape, dt))

        def sem(name):
            return ctx.enter_context(nc.semaphore(name))

        xs = sb("xs", [128, XT + 2, BATCH])
        xnat = xs[:, XT:XT + 2, :].rearrange("p a b -> p (a b)").rearrange("p (t n) -> p t n", n=RW)
        stack = sb("stack", [128, 4 * BATCH], f32r)
        kraw = sb("kraw", [128, BLK])
        khi = sb("khi", [128, KRING, BLK], f32r)
        klo = sb("klo", [128, KRING, BLK], f32r)
        prod = sb("prod", [128, PBUF, HB])
        sums = sb("sums", [128, CH])
        row_sums = sb("row_sums", [128, 2, BT, 2, NAT])
        ones = sb("ones", [128, 64])
        tps = ctx.enter_context(nc.psum_tensor("tps", [128, TBUF, HB], f32))
        rps = ctx.enter_context(nc.psum_tensor("rps", [128, 2, CH], f32))

        first_x = list(range(ROUNDS - 1, XT))
        rest_x = list(range(ROUNDS - 2, -1, -1))
        corner_loaded = [[sem(f"x_{k}_half_{h}_loaded") for h in range(2)] for k in (XT, XT + 1)]
        xnat_loaded = [sem(f"xnat_piece_{p}_loaded") for p in range(PIECES)]
        x_loaded = {k: sem(f"x_loaded_{k}") for k in first_x}
        x_rest_loaded = sem("x_rest_loaded")
        kraw_loaded = sem("kraw_loaded")
        ones_zeroed = sem("ones_zeroed")
        ones_ready = sem("ones_ready")
        khi_ready = sem("khi_ready")
        klo_ready = sem("klo_ready")
        corner_lo_ready = [sem(f"row_{FIELDS - NAT + n}_lo_ready") for n in range(CORNER_ROWS)]
        xtmp_ready = sem("xtmp_ready")
        xhi_ready = sem("xhi_ready")
        xlo_ready = sem("xlo_ready")
        t_ready = sem("t_ready")
        prod_ready = sem("prod_ready")
        tile_summed = sem("tile_summed")
        halves_added = sem("halves_added")
        row_reduced = sem("row_reduced")
        sums_copied = sem("sums_copied")
        sums_stored = sem("sums_stored")
        rows_stored = [sem("even_rows_stored"), sem("odd_rows_stored")]

        def units_before(i):
            return NU * i + CORNER_UNITS

        def blocks_before(i):
            return BLOCKS * i + 1

        def halves_before(i):
            return 8 * i + 2 * CORNER_ROWS

        def lows_before(i):
            return 8 * i

        def tiles_before(i):
            return TILES * i + CORNER_TILES

        def pieces_before(i):
            return 4 * PIECES * i

        def row_of(engine, i):
            return ROUNDS - 1 - i if isinstance(i, int) else engine.snap(i * -1 + (ROUNDS - 1))

        block = ctx.enter_context(nc.Block())

        @block.sync
        def _(sp):
            def load_weights(block):
                for top in (0, E):
                    sp.dma_start(kraw[top:top + E, :], block).then_inc(kraw_loaded, 16)

            def load_block(i, b):
                sp.wait_ge(klo_ready, blocks_before(i) + b)
                load_weights(w[i, b])

            def load_x(k):
                sp.dma_start(xs[:, k, :], x[k]).then_inc(x_loaded[k], 16)

            def load_xnat(p):
                part = slice(p * PB, (p + 1) * PB)
                sp.dma_start(xnat[:, part], xn[:, part]).then_inc(xnat_loaded[p], 16)

            def load_rest(some):
                for k in some:
                    sp.dma_start(xs[:, k, :], x[k]).then_inc(x_rest_loaded, 16)

            load_weights(wc)
            for k in range(2):
                for h in range(2):
                    b = slice(h * HB, (h + 1) * HB)
                    sp.dma_start(xs[:, k, b], x[XT + k, :, b]).then_inc(corner_loaded[k][h], 16)
            load_x(first_x[0])
            load_block(0, 0)
            load_x(first_x[1])
            load_xnat(0)
            load_x(first_x[2])
            load_block(0, 1)
            load_xnat(1)
            load_x(first_x[3])
            load_xnat(2)
            load_block(0, 2)
            load_xnat(3)
            for b, k in ((3, 4), (4, 6)):
                load_x(first_x[k])
                load_x(first_x[k + 1])
                load_block(0, b)
            sp.wait_ge(prod_ready, units_before(0))
            load_rest(rest_x[:3])
            load_block(0, 5)
            load_rest(rest_x[3:])
            for b in range(6, BLOCKS):
                load_block(0, b)
            with sp.Fori(1, ROUNDS) as i:
                for b in range(BLOCKS):
                    load_block(i, b)

        @block.scalar
        def _(act):
            def split_half(k, odd, slot, h):
                src = slice(E * odd, E * odd + E)
                dst = slice(E * (1 - odd), E * (1 - odd) + E)
                at = slot * BATCH + h * HB
                source = xs[src, k, h * HB:(h + 1) * HB]
                nc.scalar.activation(stack[src, at:at + HB], source, ACT.Copy).then_inc(xtmp_ready, 1)
                nc.scalar.activation(stack[dst, at:at + HB], source, ACT.Copy).then_inc(xhi_ready, 1)

            def even_half(i, j, n, h, first):
                if h == 0:
                    if first:
                        act.wait_ge(t_ready, CORNER_UNITS if n else 2)
                        act.wait_ge(x_loaded[ROUNDS + i if n else j], 16)
                    else:
                        act.wait_ge(t_ready, units_before(i - 1) + last_unit_of_tile(SINGLE - 1 + n) + 1)
                split_half(ROUNDS + i if n else j, 0, n, h)

            def odd_half(i, j, n, h):
                if h == 0:
                    act.wait_ge(t_ready, units_before(i))
                split_half(ROUNDS + i if n else j, 1, 2 + n, h)

            def weights(i, b, back=0):
                n = b % KRING
                act.wait_ge(kraw_loaded, 32 * (blocks_before(i) + b + 1))
                if back == "corner":
                    if n == KRING - 1:
                        act.wait_ge(t_ready, CORNER_UNITS)
                else:
                    act.wait_ge(t_ready, units_before(i - back) + last_unit_of_block((b - KRING) % BLOCKS) + 1)
                nc.scalar.activation(khi[:, n, :], kraw[:, :], ACT.Copy).then_inc(khi_ready, 1)

            def store_rows(i, odd):
                act.wait_ge(row_reduced, pieces_before(i) + 2 * PIECES * (odd + 1))
                act.dma_start(out_rows[i, odd], row_sums[:, odd]).then_inc(rows_stored[odd], 16)

            def store_sums(i, odd, first):
                act.wait_ge(tile_summed, tiles_before(i) + (TILES if odd else GROUP))
                if not first or odd:
                    act.wait_ge(sums_stored, 16 * (2 * i + odd))
                nc.scalar.activation(sums[:, :], rps[:, odd, :], ACT.Copy).then_inc(sums_copied, 1)
                act.wait_ge(sums_copied, 2 * i + odd + 1)
                act.dma_start(out[2 * i + odd], sums[:, :]).then_inc(sums_stored, 16)

            def corner():
                act.wait_ge(kraw_loaded, 32)
                nc.scalar.activation(khi[:, KRING - 1, :], kraw[:, :], ACT.Copy).then_inc(khi_ready, 1)
                for n in range(CORNER_ROWS):
                    for h in range(2):
                        act.wait_ge(corner_loaded[n // 2][h], 16)
                        split_half(n // 2, n % 2, (0, 2, 1)[n], h)
                    if n == 1:
                        weights(0, 0, "corner")

            def even_part(i, j, first):
                weights(i, 2, "corner" if first else 1)
                odd_half(i, j, 0, 0)
                if not first:
                    store_sums(i - 1, 1, False)
                    store_rows(i - 1, 1)
                weights(i, 3)
                odd_half(i, j, 0, 1)
                weights(i, 4)
                odd_half(i, j, 1, 0)
                odd_half(i, j, 1, 1)
                weights(i, 5)

            def odd_part(i, following, j, last, first=False):
                weights(i, 6)
                if not last:
                    even_half(following, j, 0, 0, False)
                store_sums(i, 0, first)
                store_rows(i, 0)
                if not last:
                    even_half(following, j, 0, 1, False)
                weights(i, 7)
                if not last:
                    even_half(following, j, 1, 0, False)
                weights(i, 8)
                if not last:
                    even_half(following, j, 1, 1, False)
                    weights(following, 0, 1)
                    weights(following, 1, 1)

            corner()
            for h in range(2):
                even_half(0, ROUNDS - 1, 0, h, True)
            weights(0, 1, "corner")
            for h in range(2):
                even_half(0, ROUNDS - 1, 1, h, True)
            even_part(0, ROUNDS - 1, True)
            act.wait_ge(x_rest_loaded, 16 * len(rest_x))
            odd_part(0, 1, ROUNDS - 2, False, True)
            even_part(1, ROUNDS - 2, False)
            with act.Fori(2, ROUNDS) as i:
                j = row_of(act, i)
                odd_part(i - 1, i, j, False)
                even_part(i, j, False)
            odd_part(ROUNDS - 1, ROUNDS, None, True)
            store_sums(ROUNDS - 1, 1, False)
            store_rows(ROUNDS - 1, 1)
            act.wait_ge(sums_stored, 16 * 2 * ROUNDS)
            for odd in range(2):
                act.wait_ge(rows_stored[odd], 16 * ROUNDS)

        @block.gpsimd
        def _(pool):
            nc.gpsimd.memset(ones[:, :], 0.0).then_inc(ones_zeroed, 1)
            pool.wait_ge(ones_zeroed, 1)
            nc.gpsimd.memset(ones[0:E, 32:33], 1.0).then_inc(ones_ready, 1)
            nc.gpsimd.memset(ones[E:2 * E, 33:34], 1.0).then_inc(ones_ready, 1)
            pool.wait_ge(ones_ready, 2)

            def low_half(k, odd, slot, h, nth, ready):
                src = slice(E * odd, E * odd + E)
                at = slot * BATCH + h * HB
                pool.wait_ge(xtmp_ready, nth)
                nc.gpsimd.tensor_tensor(stack[src, at:at + HB], xs[src, k, h * HB:(h + 1) * HB],
                                        stack[src, at:at + HB].bitcast(f32), ALU.subtract).then_inc(ready, 1)

            def even_half(i, j, n, h):
                low_half(ROUNDS + i if n else j, 0, n, h, halves_before(i) + 2 * n + h + 1, xlo_ready)

            def odd_half(i, j, n, h, blocks, pieces):
                pool.wait_ge(klo_ready, blocks)
                pool.wait_ge(halves_added, 2 * pieces)
                low_half(ROUNDS + i if n else j, 1, 2 + n, h, halves_before(i) + 4 + 2 * n + h + 1, xlo_ready)
                pool.wait_ge(xlo_ready, lows_before(i) + 4 + 2 * n + h + 1)

            def weights(n, nth):
                pool.wait_ge(khi_ready, nth)
                nc.gpsimd.tensor_tensor(klo[:, n, :], kraw[:, :], khi[:, n, :].bitcast(f32),
                                        ALU.subtract).then_inc(klo_ready, 1)

            def round_weights(i, b):
                weights(b % KRING, blocks_before(i) + b + 1)

            def piece(i, n):
                l = ROW_UNITS[n]
                v = prod[:, P_OF[l], :].rearrange("p (n o) -> p n o", o=E)
                pool.wait_ge(prod_ready, units_before(i) + l + 1)
                for m, width in enumerate((E // 2, E // 4)):
                    if m:
                        pool.wait_ge(halves_added, 2 * (4 * PIECES * i + n) + 1)
                    nc.gpsimd.tensor_tensor(v[:, :, 0:width], v[:, :, 0:width], v[:, :, width:2 * width],
                                            ALU.add).then_inc(halves_added, 1)

            def even_part(i, j):
                blocks, pieces = blocks_before(i), 4 * PIECES * i
                round_weights(i, 2)
                piece(i, 0)
                piece(i, 1)
                odd_half(i, j, 0, 0, blocks + 3, pieces + 2)
                piece(i, 2)
                piece(i, 3)
                round_weights(i, 3)
                odd_half(i, j, 0, 1, blocks + 4, pieces + 4)
                piece(i, 4)
                round_weights(i, 4)
                piece(i, 5)
                odd_half(i, j, 1, 0, blocks + 5, pieces + 6)
                piece(i, 6)
                piece(i, 7)
                odd_half(i, j, 1, 1, blocks + 5, pieces + 8)
                round_weights(i, 5)

            def odd_part(i, following, j, last):
                round_weights(i, 6)
                if not last:
                    even_half(following, j, 0, 0)
                piece(i, 8)
                piece(i, 9)
                if not last:
                    even_half(following, j, 0, 1)
                piece(i, 10)
                round_weights(i, 7)
                piece(i, 11)
                if not last:
                    even_half(following, j, 1, 0)
                round_weights(i, 8)
                piece(i, 12)
                piece(i, 13)
                if not last:
                    even_half(following, j, 1, 1)
                    round_weights(following, 0)
                piece(i, 14)
                piece(i, 15)
                if not last:
                    round_weights(following, 1)

            weights(KRING - 1, 1)
            pool.wait_ge(klo_ready, 1)
            for h in range(2):
                low_half(0, 1, 2, h, 2 + h + 1, corner_lo_ready[1])
            pool.wait_ge(corner_lo_ready[1], 2)
            round_weights(0, 0)
            even_half(0, ROUNDS - 1, 0, 0)
            even_half(0, ROUNDS - 1, 0, 1)
            round_weights(0, 1)
            even_half(0, ROUNDS - 1, 1, 0)
            even_half(0, ROUNDS - 1, 1, 1)
            even_part(0, ROUNDS - 1)
            with pool.Fori(1, ROUNDS) as i:
                j = row_of(pool, i)
                odd_part(i - 1, i, j, False)
                even_part(i, j)
            odd_part(ROUNDS - 1, ROUNDS, None, True)

        @block.tensor
        def _(pe):
            def x_parts(odd, place, j, c):
                at = 2 * odd * BATCH + c * CH + second_row(place, j) * BATCH
                return stack[:, at:at + CH] if isinstance(at, int) else stack[:, bass.ds(at, CH)]

            def half_tile(terms, h, buf):
                passes = [(part[:, n, at:at + 128], x_of) for n, at, x_of in terms for part in (khi, klo)]
                for m, (weights, x_of) in enumerate(passes):
                    for c in range(2):
                        last = nc.tensor.matmul(tps[:, buf, c * CH:(c + 1) * CH], weights, x_of(2 * h + c),
                                                start=m == 0, stop=m == len(passes) - 1)
                return last

            def stack_of(slot):
                return lambda c: stack[:, slot * BATCH + c * CH:slot * BATCH + (c + 1) * CH]

            def tile_half(j, tile, h, buf):
                if tile == SINGLE:
                    terms = [(slot_of(tile), stack_of(2)), (slot_of(tile) + 1, stack_of(1))]
                else:
                    odd = int(tile > SINGLE)
                    terms = [(slot_of(tile), lambda c: x_parts(odd, tile - (SINGLE + 1) * odd, j, c))]
                return half_tile([(slot // 4 % KRING, slot % 4 * 128, x_of) for slot, x_of in terms], h, buf)

            def row_piece(stack_slot, ring, piece, buf):
                for t in range(PB):
                    first = stack_slot * BATCH + (piece * PB + t) * 128
                    for part in (khi, klo):
                        last = nc.tensor.matmul(tps[:, buf, t * RW:(t + 1) * RW],
                                                stack[:, first:first + 128], part[:, ring, :RW],
                                                start=part is khi, stop=part is klo)
                return last

            def unit(i, j, l, first):
                kind, n, h = UNITS[l]
                back, user = user_before(l, T_OF)
                pe.wait_ge(prod_ready, CORNER_UNITS - TBUF + T_OF[l] + 1 if first and back
                           else units_before(i - back) + user + 1)
                slot = slot_of(n) if kind == "tile" else SLOTS.index(("row", n))
                if h == 0:
                    last_slot = slot + (n == SINGLE and kind == "tile")
                    pe.wait_ge(klo_ready, blocks_before(i) + last_slot // 4 + 1)
                half = h if kind == "tile" else h * 2 // PIECES
                need = None
                if kind == "row":
                    need = n
                elif n in (0, SINGLE, SINGLE + 1):
                    need = {0: 0, SINGLE: 2, SINGLE + 1: 2}[n]
                elif (n - (SINGLE + 1) * (n > SINGLE)) + ROUNDS - 1 >= PLACES:
                    need = 1 + 2 * (n > SINGLE)
                if need is not None:
                    pe.wait_ge(xhi_ready, halves_before(i) + 2 * need + half + 1)
                    pe.wait_ge(xlo_ready, lows_before(i) + 2 * need + half + 1)
                if kind == "tile":
                    last = tile_half(j, n, h, T_OF[l])
                else:
                    last = row_piece(n, slot // 4 % KRING, h, T_OF[l])
                last.then_inc(t_ready, 1)

            def sum_halves(place, odd, buffers, start, stop):
                for c in range(CHUNKS):
                    last = nc.tensor.matmul(rps[32 * c:32 * c + 32, odd, :],
                                            ones[:, 32 - 2 * place:64 - 2 * place],
                                            prod[:, buffers[c // 2], c % 2 * CH:(c % 2 + 1) * CH],
                                            start=start, stop=stop)
                last.then_inc(tile_summed, 1)

            def sum_tile(i, tile, first):
                odd = int(tile > SINGLE)
                place = tile - GROUP * odd
                if place == 0 and not first:
                    pe.wait_ge(sums_copied, 2 * i - 1 + odd)
                l = last_unit_of_tile(tile)
                pe.wait_ge(prod_ready, units_before(i) + l + 1)
                sum_halves(place, odd, P_OF[l - 1:l + 1], place == 0 and not (first and odd),
                           place == GROUP - 1 - odd)

            def sum_corner(tile):
                pe.wait_ge(prod_ready, 2 * tile + 2)
                sum_halves(PLACES + tile, 1, (2 * tile, 2 * tile + 1), tile == 0, False)

            def sums_due(i, l, first):
                for tile in TILE_ORDER:
                    if last_unit_of_tile(tile) + SUM_LAG == l:
                        sum_tile(i, tile, first)

            def round_(i, j, first):
                for l in range(NU):
                    unit(i, j, l, first)
                    if not first:
                        sums_due(i - 1, l + NU, False)
                    elif l + 1 == SUM_LAG:
                        sum_corner(CORNER_TILES - 1)
                    sums_due(i, l, first)

            corner_terms = [[(0, 0)], [(1, 2)], [(2, 2), (3, 1)]]
            for n in range(CORNER_UNITS):
                tile, h = n // 2, n % 2
                if n >= TBUF:
                    pe.wait_ge(prod_ready, n - TBUF + 1)
                pe.wait_ge(klo_ready, 1)
                pe.wait_ge(xhi_ready, n + 1)
                pe.wait_ge(corner_lo_ready[tile], h + 1)
                half_tile([(KRING - 1, slot * 128, stack_of(at)) for slot, at in corner_terms[tile]],
                          h, n % TBUF).then_inc(t_ready, 1)
                if n == 0:
                    pe.wait_ge(ones_ready, 2)
                if n > SUM_LAG and h:
                    sum_corner((n - SUM_LAG) // 2)
            round_(0, ROUNDS - 1, True)
            with pe.Fori(1, ROUNDS) as i:
                j = row_of(pe, i)
                round_(i, j, False)
            sum_tile(ROUNDS - 1, TILES - 1, False)

        @block.vector
        def _(dve):
            def reduce_row(buf, row, piece):
                v = prod[:, buf, :].rearrange("p (t c o) -> p t c o", c=NAT, o=E)[:, :, :, 0:E // 4]
                nc.vector.tensor_reduce(row_sums[:, row // 2, piece * PB:(piece + 1) * PB, row % 2, :], v,
                                        AX.X, ALU.add).then_inc(row_reduced, 1)

            def multiply_row(piece, tbuf, pbuf):
                v = xnat[:, piece * PB:(piece + 1) * PB, :].rearrange("p t n -> p (t n)")
                nc.vector.tensor_tensor(prod[:, pbuf, :], tps[:, tbuf, :], v, ALU.mult).then_inc(prod_ready, 1)

            def multiply_single(top, low, b, tbuf, pbuf):
                for rows, k in ((slice(0, E), top), (slice(E, 2 * E), low)):
                    last = nc.vector.tensor_tensor(prod[rows, pbuf, :], tps[rows, tbuf, :], xs[rows, k, b],
                                                   ALU.mult)
                return last

            def multiply_half(i, j, tile, h, tbuf, pbuf):
                b = slice(h * HB, (h + 1) * HB)
                if tile == SINGLE:
                    last = multiply_single(j, ROUNDS + i, b, tbuf, pbuf)
                else:
                    place = tile if tile < SINGLE else tile - SINGLE - 1
                    second = second_row(place, j)
                    k = j + (place + 1) if isinstance(second, int) and not second else \
                        (j * (second * -1 + 1) + (place + 1)) % (XT + 2)
                    last = nc.vector.tensor_tensor(prod[:, pbuf, :], tps[:, tbuf, :], xs[:, k, b], ALU.mult)
                last.then_inc(prod_ready, 1)

            def unit(i, j, l, first):
                kind, n, h = UNITS[l]
                back, user = user_before(l, P_OF)
                if first and back:
                    if P_OF[l] < CORNER_UNITS:
                        dve.wait_ge(tile_summed, P_OF[l] // 2 + 1)
                else:
                    if UNITS[user][0] == "tile":
                        nth = TILE_ORDER.index(UNITS[user][1]) + 1
                        dve.wait_ge(tile_summed, tiles_before(i - back) + nth)
                    else:
                        dve.wait_ge(row_reduced, pieces_before(i - back) + ROW_UNITS.index(user) + 1)
                dve.wait_ge(t_ready, units_before(i) + l + 1)
                if kind == "tile":
                    multiply_half(i, j, n, h, T_OF[l], P_OF[l])
                else:
                    multiply_row(h, T_OF[l], P_OF[l])

            def reduce_due(i, l, first):
                due = l - ROW_LAG
                if due in ROW_UNITS:
                    _, row, piece = UNITS[due]
                    n = ROW_UNITS.index(due)
                    if n in (0, 2 * PIECES) and not first:
                        dve.wait_ge(rows_stored[row // 2], 16 * i)
                    dve.wait_ge(halves_added, 2 * (4 * PIECES * i + n + 1))
                    reduce_row(P_OF[due], row, piece)

            def round_(i, j, first):
                for l in range(NU):
                    reduce_due(i, l, first)
                    kind, n, h = UNITS[l]
                    if first and kind == "tile" and h == 0 and n + 1 < len(first_x):
                        dve.wait_ge(x_loaded[first_x[n + 1]], 16)
                    if first and kind == "row" and n == 0:
                        dve.wait_ge(xnat_loaded[h], 16)
                    unit(i, j, l, first)

            def corner_low(n, h):
                at = n * BATCH + h * HB
                dve.wait_ge(xtmp_ready, 4 * n + h + 1)
                nc.vector.tensor_tensor(stack[0:E, at:at + HB], xs[0:E, n, h * HB:(h + 1) * HB],
                                        stack[0:E, at:at + HB].bitcast(f32), ALU.subtract)\
                    .then_inc(corner_lo_ready[2 * n], 1)

            def corner_unit(n):
                tile, h = n // 2, n % 2
                b = slice(h * HB, (h + 1) * HB)
                dve.wait_ge(t_ready, n + 1)
                dve.wait_ge(corner_loaded[1][h], 16)
                if tile == CORNER_TILES - 1:
                    last = multiply_single(0, 1, b, n % TBUF, n)
                else:
                    last = nc.vector.tensor_tensor(prod[:, n, :], tps[:, n % TBUF, :], xs[:, 1, b], ALU.mult)
                last.then_inc(prod_ready, 1)

            corner_low(0, 0)
            corner_low(0, 1)
            for n in range(CORNER_UNITS):
                if n in (2, 3):
                    corner_low(1, n - 2)
                corner_unit(n)
            dve.wait_ge(x_loaded[first_x[0]], 16)
            round_(0, ROUNDS - 1, True)
            dve.wait_ge(x_rest_loaded, 16 * len(rest_x))
            with dve.Fori(1, ROUNDS) as i:
                j = row_of(dve, i)
                round_(i, j, False)


def tiles_of_round(i):
    j = ROUNDS - 1 - i
    even = [(2 * j, k) for k in range(j + 1, XT)] + [(2 * (XT - 1 - j), k) for k in range(XT - j, XT)]
    return even, [(r + 1, k) for r, k in even]


def rows_of_round(i):
    j = ROUNDS - 1 - i
    return 2 * j, 2 * (XT - 1 - j), 2 * j + 1, 2 * (XT - 1 - j) + 1


def pair_number(r, c):
    return r * FIELDS - r * (r + 1) // 2 + c - r - 1


def kernel(r_x, L0_rec_kernel):
    import numpy as np
    import concourse.bacc as bacc
    from concourse.bass_utils import run_bass_kernel_spmd

    x = np.asarray(r_x)
    wk = np.asarray(L0_rec_kernel)
    xt = np.ascontiguousarray(x.transpose(1, 2, 0)).reshape(FIELDS // 2, 2 * E, BATCH)
    xn = np.ascontiguousarray(x[:, FIELDS - NAT:].reshape(BT, 128, RW).transpose(1, 0, 2))
    by_in = wk.transpose(2, 1, 0)
    by_out = wk.transpose(0, 1, 2)
    wt = np.zeros((ROUNDS, E, 4 * BLOCKS, 2, E), wk.dtype)
    wc = np.zeros((E, 4, 2, E), wk.dtype)
    order = np.zeros((2 * ROUNDS, 16, 2), np.int64) - 1
    row_order = np.zeros((ROUNDS, 2, 2, NAT), np.int64) - 1
    last_fields = range(FIELDS - NAT, FIELDS)
    for i in range(ROUNDS):
        j = ROUNDS - 1 - i
        for odd, tiles in enumerate(tiles_of_round(i)):
            for s, (r, k) in enumerate(tiles):
                for m in range(2):
                    n = pair_number(r, 2 * k + m)
                    wt[i, :, slot_of(s + (SINGLE + 1) * odd), m] = by_in[:, n]
                    order[2 * i + odd, s, m] = n
        top = pair_number(2 * j, 2 * j + 1)
        low = pair_number(2 * (XT - 1 - j), 2 * (XT - 1 - j) + 1)
        wt[i, :, slot_of(SINGLE), 0] = by_out[:, top]
        wt[i, :, slot_of(SINGLE) + 1, 1] = by_in[:, low]
        order[2 * i, SINGLE] = top, low
        for row, r in enumerate(rows_of_round(i)):
            for m, c in enumerate(last_fields):
                n = pair_number(r, c)
                wt[i, :, SLOTS.index(("row", row)) + m // 2, m % 2] = by_in[:, n]
                row_order[i, row // 2, row % 2, m] = n
    a = FIELDS - NAT
    for slot in range(2):
        for m in range(2):
            n = pair_number(a + slot, a + 2 + m)
            wc[:, slot, m] = by_in[:, n]
            order[1, PLACES + slot, m] = n
    for m in range(2):
        n = pair_number(a + 2 * m, a + 2 * m + 1)
        wc[:, 2 + m, m] = (by_in if m else by_out)[:, n]
        order[1, PLACES + 2, m] = n
    wt = np.ascontiguousarray(wt.reshape(ROUNDS, E, BLOCKS, BLK).transpose(0, 2, 1, 3))
    wc = wc.reshape(E, BLK)

    f32 = mybir.dt.float32
    nc = bacc.Bacc("TRN2", target_bir_lowering=False, num_devices=1)
    arrays = {"x_t": xt, "x_nat": xn, "w_t": wt, "w_corner": wc}
    args = [nc.dram_tensor(name, a.shape, f32, kind="ExternalInput").ap() for name, a in arrays.items()]
    args += [nc.dram_tensor("sums_t", (2 * ROUNDS, 128, CH), f32, kind="ExternalOutput").ap(),
             nc.dram_tensor("row_sums_t", (ROUNDS, 2, 128, BT, 2, NAT), f32, kind="ExternalOutput").ap()]
    build(nc, *args)
    got = run_bass_kernel_spmd(nc, [arrays], core_ids=[0]).results[0]
    tiles = np.asarray(got["sums_t"]).reshape(2 * ROUNDS, CHUNKS, 32, CH).transpose(1, 3, 0, 2).reshape(BATCH, -1)
    rows = np.asarray(got["row_sums_t"]).transpose(3, 2, 0, 1, 4, 5).reshape(BATCH, -1)
    result = np.empty((BATCH, PAIRS), x.dtype)
    for source, where in ((tiles, order.reshape(-1)), (rows, row_order.reshape(-1))):
        result[:, where[where >= 0]] = source[:, where >= 0]
    return result
```
